# Optimizing a Trainium2 kernel written in Bass

```python
import numpy as np
import jax
import jax.numpy as jnp

def _softmax(x, axis=-1):
    return jax.nn.softmax(x, axis=axis)

def _gelu(x):
    return jax.nn.gelu(x, approximate=True)

def _silu(x):
    return jax.nn.silu(x)

def _sigmoid(x):
    return jax.nn.sigmoid(x)

def _layernorm(x, axis=-1, eps=1e-05):
    m = jnp.mean(x, axis=axis, keepdims=True)
    v = jnp.var(x, axis=axis, keepdims=True)
    return (x - m) / jnp.sqrt(v + eps)

def _scatter_add(tgt, idx, src, axis=0):
    return tgt.at[idx].add(src)

def _segment_sum(src, seg, n):
    return jax.ops.segment_sum(src, seg, n)
kernel_name = 'mk_prb_d1_jaxref_r8_7d2753'

def setup_inputs(seed: int=0):
    np.random.seed(seed)
    _w = jnp.asarray

    def _L0_attn_setup():
        import jax, jax.numpy as jnp
        import numpy as np
        N_HEADS = 16
        key = jax.random.key(seed)
        ks = jax.random.split(key, 9)
        B, S, D = (2, 256, 256)
        s = 0.02
        return {'X': jax.random.normal(ks[0], (B, S, D), jnp.float32), 'Wq': jax.random.normal(ks[1], (D, D), jnp.float32) * s, 'bq': jax.random.normal(ks[2], (D,), jnp.float32) * s, 'Wk': jax.random.normal(ks[3], (D, D), jnp.float32) * s, 'bk': jax.random.normal(ks[4], (D,), jnp.float32) * s, 'Wv': jax.random.normal(ks[5], (D, D), jnp.float32) * s, 'bv': jax.random.normal(ks[6], (D,), jnp.float32) * s, 'Wo': jax.random.normal(ks[7], (D, D), jnp.float32) * s, 'bo': jax.random.normal(ks[8], (D,), jnp.float32) * s}
    _L0_attn_in = _L0_attn_setup()

    def _L0_ffn_setup():
        import jax, jax.numpy as jnp
        import numpy as np
        RANK = 64
        SCALING = 1.0 / RANK
        TEMPERATURE = 1.0
        key = jax.random.key(seed)
        k_x, k_a, k_b, k_w = jax.random.split(key, 4)
        B_, S, D = (4, 256, 256)
        E, R, O = (8, RANK, 256)
        x = jax.random.normal(k_x, (B_, S, D), dtype=jnp.float32)
        A = jax.random.normal(k_a, (E, R, D), dtype=jnp.float32) * (1.0 / np.sqrt(D))
        Bw = jax.random.normal(k_b, (E, O, R), dtype=jnp.float32) * 0.02
        Wr = jax.random.normal(k_w, (E, D), dtype=jnp.float32) * (1.0 / np.sqrt(D))
        br = jnp.zeros((E,), dtype=jnp.float32)
        return {'x': x, 'A': A, 'B': Bw, 'Wr': Wr, 'br': br}
    _L0_ffn_in = _L0_ffn_setup()
    _d = {'L0_attn_X': _L0_attn_in['X'], 'L0_attn_Wq': _L0_attn_in['Wq'], 'L0_attn_bq': _L0_attn_in['bq'], 'L0_attn_Wk': _L0_attn_in['Wk'], 'L0_attn_bk': _L0_attn_in['bk'], 'L0_attn_Wv': _L0_attn_in['Wv'], 'L0_attn_bv': _L0_attn_in['bv'], 'L0_attn_Wo': _L0_attn_in['Wo'], 'L0_attn_bo': _L0_attn_in['bo'], 'L0_ffn_A': _L0_ffn_in['A'], 'L0_ffn_B': _L0_ffn_in['B'], 'L0_ffn_Wr': _L0_ffn_in['Wr'], 'L0_ffn_br': _L0_ffn_in['br']}
    _x0 = _d['L0_attn_X']
    _d['L0_attn_X'] = jax.random.normal(jax.random.fold_in(jax.random.key(seed), 1), (1, 1024, 256), dtype=_x0.dtype)
    del _x0
    return _d

def reference(L0_attn_X, L0_attn_Wq, L0_attn_bq, L0_attn_Wk, L0_attn_bk, L0_attn_Wv, L0_attn_bv, L0_attn_Wo, L0_attn_bo, L0_ffn_A, L0_ffn_B, L0_ffn_Wr, L0_ffn_br):

    def _L0_attn_ref(X, Wq, bq, Wk, bk, Wv, bv, Wo, bo):
        import jax, jax.numpy as jnp
        import numpy as np
        N_HEADS = 16
        B, S, D = X.shape
        H = N_HEADS
        d_head = D // H
        scale = jnp.asarray(1.0 / np.sqrt(np.sqrt(d_head)), X.dtype)
        Q = (X @ Wq.T + bq).reshape(B, S, H, d_head) * scale
        K = (X @ Wk.T + bk).reshape(B, S, H, d_head) * scale
        V = (X @ Wv.T + bv).reshape(B, S, H, d_head)
        scores = jnp.einsum('bqhd,bkhd->bhqk', Q, K)
        causal = jnp.tril(jnp.ones((S, S), bool))
        scores = jnp.where(causal[None, None], scores, -jnp.inf)
        attn = jax.nn.softmax(scores.astype(jnp.float32), axis=-1).astype(X.dtype)
        out = jnp.einsum('bhqk,bkhd->bqhd', attn, V).reshape(B, S, D)
        return out @ Wo.T + bo

    def _L0_ffn_ref(x, A, B, Wr, br):
        import jax, jax.numpy as jnp
        import numpy as np
        RANK = 64
        SCALING = 1.0 / RANK
        TEMPERATURE = 1.0
        batch, seq, d = x.shape
        E, out_dim = (B.shape[0], B.shape[1])
        x_flat = x.reshape(-1, d)
        logits = (x_flat @ Wr.T + br) / TEMPERATURE
        probs = jax.nn.softmax(logits, axis=-1)
        expert_idx = jnp.argmax(probs, axis=-1)
        expert_weight = jnp.max(probs, axis=-1)
        h = jnp.einsum('nd,erd->ner', x_flat, A)
        y = jnp.einsum('ner,eor->neo', h, B) * SCALING
        sel = jnp.take_along_axis(y, expert_idx[:, None, None], axis=1)[:, 0, :]
        out_flat = sel * expert_weight[:, None]
        return out_flat.reshape(batch, seq, out_dim)
    x = L0_attn_X
    xn = _layernorm(x, axis=-1)
    x = x + _L0_attn_ref(xn, L0_attn_Wq, L0_attn_bq, L0_attn_Wk, L0_attn_bk, L0_attn_Wv, L0_attn_bv, L0_attn_Wo, L0_attn_bo) + _L0_ffn_ref(xn, L0_ffn_A, L0_ffn_B, L0_ffn_Wr, L0_ffn_br)
    return x

_drawn_inputs = setup_inputs


def setup_inputs(seed=0):
    import zlib

    import numpy as np

    out = dict(_drawn_inputs(seed))
    spreads = {'L0_ffn_br': (0.0, 2.0)}
    factors = {'L0_attn_Wq': 8.0,
     'L0_attn_bq': 8.0,
     'L0_attn_Wk': 8.0,
     'L0_attn_bk': 64.0,
     'L0_attn_Wv': 6.465,
     'L0_attn_bv': 8.0,
     'L0_attn_Wo': 5.095,
     'L0_attn_bo': 7.977,
     'L0_ffn_A': 8.0,
     'L0_ffn_B': 8.0,
     'L0_ffn_Wr': 8.0}
    for name, (base, spread) in spreads.items():
        noise = np.random.default_rng([zlib.crc32(name.encode()), seed]).standard_normal(out[name].shape)
        drawn = base * np.exp(spread * noise) if base else spread * noise
        out[name] = jnp.asarray(drawn.astype(out[name].dtype))
    for name, factor in factors.items():
        out[name] = (out[name] * factor).astype(out[name].dtype)
    return out
```

```python
from contextlib import ExitStack

import concourse.bass as bass
from concourse import mybir

F32 = mybir.dt.float32
BF16 = mybir.dt.bfloat16
F32R = mybir.dt.float32r
ALU = mybir.AluOpType
ACT = mybir.ActivationFunctionType
AX = mybir.AxisListType

P = 128
LOW = -3.0e38
EPS = 1e-5


def layer_kernel(nc, X, Wq, bq, Wk, bk, Wv, bv, Wo, bo, A, B, Wr, br, out):
    _, S, D = X.shape
    E, R, _ = A.shape
    H = 16
    DH = D // H
    SCALE = DH ** -0.25
    T = S // P
    C = D // P
    ER = E * R
    ERC = ER // P
    HALF = S // 2
    HB = HALF // P
    G = 4
    PARTS = 6
    KR = PARTS * DH
    MR = KR + 2
    VW = 32
    NP = 3
    LAG = 2

    units = [(0, 0), (1, 0), (0, 1), (1, 1), (2, 1), (3, 1), (2, 0), (3, 0)]
    NU = len(units)
    steps = [(u, kb) for u, (g, j) in enumerate(units) for kb in range(HB * (j + 1))]
    NS = len(steps)
    quarters = sorted((max(u for u, (g, half) in enumerate(units) if half == j and g * C // G == c), j, c)
                      for j in range(2) for c in range(C))
    NQ = len(quarters)

    def share_of(k):
        u, j, c = quarters[k // 2]
        return k // 2, j, c, j * HB + 2 * (k % 2)
    first_step = [min(s for s in range(NS) if steps[s][0] == u) for u in range(NU)]
    last_step = [max(s for s in range(NS) if steps[s][0] == u) for u in range(NU)]
    diagonal = [kb >= HB * units[u][1] for u, kb in steps]
    hidden_before = [sum(diagonal[:s]) for s in range(NS + 1)]

    mx_tiles = []
    for u, (g, j) in enumerate(units):
        for qb in range(HB * j, HB * j + HB):
            for h in range(G):
                if j:
                    mx_tiles.append((u, qb, h, 0, HALF))
                mx_tiles.append((u, qb, h, HALF * j, P * (qb - HB * j + 1)))
    mx_end = [max(i for i, t in enumerate(mx_tiles) if t[0] == u) + 1 for u in range(NU)]

    fills = [("wk", 0), ("x", 0), ("x", 1), ("wq", 0), ("kq", 0), ("wr", 0), ("x", 2), ("x", 3), ("kq", 1),
             ("wo", 0), ("kq", 2), ("lt", 0), ("bt", 0), ("wv", 0), ("lg", 0), ("kq", 3), ("v", 0), ("bt", 1),
             ("v", 1), ("v", 2), ("at", 0), ("at", 1), ("v", 3)]
    N_PRE = len(fills)
    NB = 4
    fills += [("kq", 4), ("h", 0), ("h", 1), ("ht", 0), ("kq", 5), ("ht", 1), ("kq", 6), ("h", 2), ("y", 0),
              ("kq", 7), ("h", 3), ("ht", 2), ("y", 1), ("ht", 3), ("h", 4), ("y", 2), ("h", 5), ("ht", 4),
              ("y", 3), ("h", 6), ("ht", 5), ("y", 4), ("ht", 6), ("h", 7), ("y", 5), ("ht", 7), ("y", 6),
              ("y", 7)]
    SPLIT = ("wk", "wq", "wv", "x", "at")
    reader = {"wk": "dve", "wq": "dve", "x": "dve", "kq": "act", "wr": "act", "lt": "act", "lg": "dve", "wv": "dve",
              "at": "dve", "v": "dve", "bt": "act", "wo": "act", "h": "dve", "ht": "act", "y": "dve"}

    def read_by(i):
        who = reader[fills[i][0]]
        return who, sum(reader[f[0]] == who for f in fills[:i + 1])

    at_fill = {f: i for i, f in enumerate(fills)}
    split_fills = [f for f in fills if f[0] in SPLIT]

    kq_items = [(w, c, j) for c in range(C) for j in range(2) for w in ("k", "q")]

    def stacks_of(u):
        g, j = units[u]
        return [i for i, (w, c, jj) in enumerate(kq_items) if c == g * G // 8 and (jj == j or (jj < j and w == "k"))]

    pe_jobs = []
    late = fills[N_PRE:]
    now = {"pe": 8000.0, "dve": 0.0, "act": 0.0, "misc": 0.0}
    taken, exp_end, m_ready, split_at, stack_at = [], {}, {}, {}, {}
    PARTS_OF = {"kq": 3, "h": 3, "y": 4}
    rows_due = []

    def engine(who, since, length):
        now[who] = max(now[who], since) + length
        return now[who]

    def start_of(what, k):
        t = now["pe"]
        if what == "st":
            s, hp = k
            t = max(t, exp_end.get((s - 1, hp), 0))
            if s == first_step[steps[s][0]] and hp == 0:
                t = max(t, m_ready[steps[s][0]])
        elif what == "pv":
            t = max(t, exp_end[(k[0], 1)] + (500 if diagonal[k[0]] else 0))
        elif what == "mx":
            t = max([t] + [stack_at.get(i, 1e9) for i in stacks_of(mx_tiles[k[0]][0])] + taken[-2:-1])
        elif what == "m":
            t = max(t, split_at[k[0]] + 60, now["misc"])
        elif what in ("late", "turn", "hT", "out"):
            t = max(t, now["misc"])
        return t

    def put(what, k):
        if what == "part":
            pe_jobs.append((what, k))
            now["pe"] = start_of("late" if k[1] == 0 else what, k)
            engine("pe", 0, {"kq": 1290, "h": 1290, "y": 1720}[k[0][0]] // PARTS_OF[k[0][0]])
            while len(taken) < len(mx_tiles) and start_of("mx", (len(taken),)) <= now["pe"] + SLACK \
                    and all(i in stack_at for i in stacks_of(mx_tiles[len(taken)][0])):
                put("mx", (len(taken),))
            return
        n_parts = PARTS_OF.get(k[0][0], 1) if what == "fill" and at_fill[k[0]] >= N_PRE else 1
        for n in range(n_parts - 1):
            put("part", (k[0], n))
        now["pe"] = start_of("late" if what == "fill" and at_fill[k[0]] >= N_PRE and n_parts == 1 else what, k)
        pe_jobs.append((what, k))
        if what == "st":
            w = HALF - P * max(0, steps[k[0]][1] - HB * units[steps[k[0]][0]][1])
            exp_end[k] = engine("act", engine("pe", 0, 2 * w / 2.4) + 70, 120 + 2 * w / 1.2)
        elif what == "pv":
            u, kb = steps[k[0]]
            engine("pe", 0, 4 * (HALF - P * max(0, kb - HB * units[u][1])) / 2.2)
            if k[0] == last_step[u]:
                engine("act", now["pe"], 480)
        elif what == "mx":
            u, w = mx_tiles[k[0]][0], mx_tiles[k[0]][4]
            taken.append(engine("dve", engine("pe", 0, w / 2.4) + 70, 75 + w / 0.96))
            if k[0] + 1 == mx_end[u]:
                split_at[u] = engine("dve", 0, 450)
                rows_due.append(u)
        elif what == "m":
            now["misc"] = engine("act", engine("pe", 0, 220) + 70, 480)
            m_ready[k[0]] = now["misc"] + 2800
        elif what == "turn":
            now["misc"] = engine("dve", engine("pe", 0, 220) + 70, 600)
        elif what == "hT":
            now["misc"] = engine("act", engine("pe", 0, 220) + 70, 480)
        elif what == "out":
            now["misc"] = engine("dve", engine("pe", 0, 860) + 70, 600)
        elif what == "fill":
            kind, i = k[0]
            length = {"kq": 1290, "v": 1290, "h": 1290, "y": 1720, "lt": 1100}.get(kind, 220) // n_parts
            end = engine("pe", 0, length) + 70
            if kind in SPLIT or kind == "kq":
                end = engine("act", end, 1150 if kind == "kq" else 480)
                end = engine("dve", 0 if kind == "kq" and i > 3 else end, 1800 if kind == "kq" else 600)
                if kind == "kq":
                    stack_at[i] = end + 6000
            else:
                end = engine(reader[kind], end, 600 if reader[kind] == "dve" else 480)
            if at_fill[k[0]] >= N_PRE:
                now["misc"] = end - (1800 if kind == "kq" else 0)

    def between(start=None, by=0):
        while True:
            n = len(taken)
            t = now["pe"]
            until = start() if start else t
            tile = start_of("mx", (n,)) if n < len(mx_tiles) and all(
                i in stack_at for i in stacks_of(mx_tiles[n][0])) else None
            if rows_due and start_of("m", (rows_due[0],)) <= t + 30:
                put("m", (rows_due.pop(0),))
            elif tile is not None and tile <= t + SLACK:
                put("mx", (n,))
            elif late and now["misc"] <= t + SLACK and (len(late) > by or until > t + STALL):
                put("fill", (late.pop(0),))
            elif tile is not None and tile <= until:
                put("mx", (n,))
            else:
                return

    STALL = 100
    SLACK = 60
    LATE_TO = NS - 4
    n_late = len(late)
    for i, f in enumerate(fills[:N_PRE]):
        put("fill", (f,))
        between(by=n_late)
    END = NS + 8
    turn_at = {last_step[u] + 3: u for u in range(NU)}
    hT_at, out_at = {}, {}
    for n, (u, j, c) in enumerate(quarters):
        tail = 0 if u == NU - 1 else 1
        hT_at.setdefault(last_step[u] + 3 + tail, []).append(n)
        for i in range(2):
            out_at.setdefault(last_step[u] + 3 + tail * (2 + i), []).append(2 * n + i)
    for s in range(END):
        if s < NS and s == first_step[steps[s][0]]:
            u = steps[s][0]
            while u not in m_ready:
                if u in rows_due:
                    between(lambda: start_of("m", (u,)), by=n_late)
                    if u in rows_due:
                        rows_due.remove(u)
                        put("m", (u,))
                elif not all(i in stack_at for i in stacks_of(u)) or (
                        late and now["misc"] <= now["pe"] + SLACK
                        and start_of("mx", (len(taken),)) > now["pe"] + STALL):
                    put("fill", (late.pop(0),))
                else:
                    put("mx", (len(taken),))
        by = n_late * max(0, LATE_TO - s) // LATE_TO
        work = [("st", (s, 0)), ("st", (s, 1))] if s < NS else []
        if LAG <= s < NS + LAG:
            work.append(("pv", (s - LAG,)))
        if s in turn_at:
            work.append(("turn", (turn_at[s],)))
        work += [("hT", (n,)) for n in hT_at.get(s, [])] + [("out", (n,)) for n in out_at.get(s, [])]
        for what, k in work:
            between(lambda: start_of(what, k), by)
            put(what, k)
    assert len(taken) == len(mx_tiles) and not late
    misc_uses = [(w, k[0]) for w, k in pe_jobs if w in ("m", "turn", "hT") or (w == "out" and k[0] < 2 * NQ - 2)
                 or (w == "fill" and at_fill[k[0]] >= N_PRE)]

    cuts_due, gets_due = [], []
    dve_jobs = [("stats", (0,)), ("norm_x", (0,)), ("stats", (1,))]
    dma_jobs = []

    def cut_now(i):
        dve_jobs.append(("cut", (i,)))
        dma_jobs.append(("put", i))
        gets_due.append(i)

    def get_all_but(n):
        while len(gets_due) > n:
            dma_jobs.append(("get", gets_due.pop(0)))

    for w, k in pe_jobs:
        if w == "fill":
            what, i = k[0]
            if cuts_due:
                cut_now(cuts_due.pop())
                get_all_but(1)
            elif at_fill[k[0]] >= N_PRE:
                get_all_but(0)
            if what == "kq" and at_fill[k[0]] < N_PRE:
                cut_now(i)
                get_all_but(0 if i % 2 else 1)
            elif what == "kq":
                cuts_due.append(i)
            elif what in SPLIT:
                dve_jobs.append(("low", (k[0],)))
                if k[0] == ("x", 1):
                    dve_jobs.append(("norm_x", (1,)))
            elif what == "lg":
                dve_jobs.append(("lg", ()))
            elif what in ("v", "h", "y"):
                dve_jobs.append((what, (i,)))
            if k[0] == ("v", 2):
                dve_jobs.append(("choice", ()))
        elif w == "mx":
            needed = stacks_of(mx_tiles[k[0]][0])
            if any(i in cuts_due for i in needed):
                cut_now(cuts_due.pop())
            if any(i in gets_due for i in needed):
                get_all_but(0)
            dve_jobs.append((w, k))
        elif w == "out":
            dve_jobs.append((w, k))
        elif w == "turn":
            dve_jobs.append(("norm", k))
        elif w == "m":
            dma_jobs.append(("m", k[0]))

    act_jobs = [("std", 0)]
    for w, k in pe_jobs:
        if w == "fill":
            if k[0] in split_fills:
                act_jobs.append(("high", k[0]))
                if k[0] == ("wq", 0):
                    act_jobs.append(("std", 1))
            elif reader[k[0][0]] == "act":
                act_jobs.append(("fill", k[0]))
            if k[0] == ("v", 2):
                act_jobs.append(("exp_router", 0))
        elif w == "m":
            act_jobs.append(("m", k[0]))
        elif w == "st":
            act_jobs.append(("exp", k))
        elif w == "hT":
            act_jobs.append(("hT", k[0]))
        elif w == "pv" and k[0] == last_step[steps[k[0]][0]]:
            act_jobs.append(("acc", steps[k[0]][0]))

    with ExitStack() as ctx:
        def sb(name, shape, dt=F32):
            return ctx.enter_context(nc.sbuf_tensor(name, shape, dt))

        def sem(name):
            return ctx.enter_context(nc.semaphore(name))

        x_sb = sb("x_sb", [P, T, D])
        xn_sb = sb("xn_sb", [P, T, D])
        xnT = [sb(f"xnT{n}", [P, C, S], F32R) for n in range(2)]
        w_T = {w: [sb(f"{w}_T{n}", [P, C, D], F32R) for n in range(2)] for w in ("wk", "wq", "wv")}
        a_T = [sb(f"a_T{n}", [P, C, ER], F32R) for n in range(2)]
        wo_T = sb("wo_T", [P, C, D])
        b_T = sb("b_T", [P, ERC, D])
        early = sb("early", [P, 2, HALF])
        bv_all, bo_all = early[:, 0, 0:D], early[:, 0, D:2 * D]
        wr_raw, lgT = early[0:E, 1, 0:D], early[:, 1, D:D + S // 4]
        acc_sb = early
        wr_T = sb("wr_T", [P, C, VW])
        prob = sb("prob", [P, NP, G, HALF])
        space = prob[:].rearrange("p a h n -> p (a h n)")
        w_raw = {n: space[:, i * C * D:(i + 1) * C * D].rearrange("p (c n) -> p c n", c=C)
                 for i, n in enumerate(("wk", "wq", "wv", "wo"))}
        a_raw = space[:, 4 * C * D:4 * C * D + ERC * D].rearrange("p (c n) -> p c n", c=ERC)
        b_raw = space[:, 4 * C * D + ERC * D:4 * C * D + 2 * ERC * D].rearrange("p (c e r) -> p c e r", c=C, e=E)
        bias_k = sb("bias_k", [P, C])
        bias_q = sb("bias_q", [P, C])
        half_bias = {"k": sb("half_bk", [P, C]), "q": sb("half_bq", [P, C])}
        br_all = sb("br_all", [P, E])
        ident = sb("ident", [P, P])
        ident_bf = sb("ident_bf", [P, P], BF16)
        causal = sb("causal", [P, HALF])
        prio = sb("prio", [P, E])
        stats = sb("stats", [P, T, 6])
        mv = sb("mv", [P, T, 2])
        veps = sb("veps", [P, T])
        std = sb("std", [P, T])
        rstd = sb("rstd", [P, T])
        nmr = sb("nmr", [P, T])
        full = sb("full", [P, 2, HALF])
        rest = sb("rest", [P, 2, HALF])
        NPT = 3
        parts = sb("parts", [P, NPT, 3, HALF], BF16)
        stack = {"k": sb("k_stack", [P, H, S], BF16), "q": sb("q_stack", [P, H, S], BF16)}
        v_aug = sb("v_aug", [P, T, H, VW])
        heads = xn_sb
        hm = sb("hm", [P, 2, ER])
        hmT = sb("hmT", [P, 2, ERC, P])
        headsT = sb("headsT", [P, 2, HALF])
        masked = sb("masked", [P, 2, HALF], BF16)
        pm = sb("pm", [P, 2, 2, G, HB])
        mpart = sb("mpart", [P, 2, HB, 2, G], BF16)
        mrow = sb("mrow", [2 * G, 2, HALF], BF16)
        rsum = sb("rsum", [P, HB, G])
        lg = sb("lg", [P, T, E])
        ex = sb("ex", [P, T, E])
        cand = sb("cand", [P, T, E])
        onehot = sb("onehot", [P, T, E])
        r1 = sb("r1", [P, T])
        r2 = sb("r2", [P, T])
        r3 = sb("r3", [P, T])
        wgt = sb("wgt", [P, T])

        bank = [ctx.enter_context(nc.psum_tensor(f"bank{i}", [P, 512], F32)) for i in range(4)]
        mx_bank = bank[0:2]
        acc_bank = bank[2]
        misc = bank[3]

        def out_bank(n):
            return misc if n < 2 * NQ - 2 else mx_bank[n % 2]

        st = [ctx.enter_context(nc.psum_tensor(f"st{i}", [P, 2, 512], F32)) for i in range(2)]
        fill_bank = [st[0][:, 0, :], st[0][:, 1, :], st[1][:, 0, :], st[1][:, 1, :]]

        def bank_of(i):
            return fill_bank[i % NB] if i < N_PRE else misc[:]

        def halves(f):
            what, i = f
            if what == "x":
                c, j = i % 2, i // 2
                return [x[:, c, j * HALF:(j + 1) * HALF] for x in xnT]
            if what == "at":
                return [x[:, i, :] for x in a_T]
            return [x[:].rearrange("p c n -> p (c n)") for x in w_T[what]]

        scratch = nc.dram_tensor("stack_scratch", (2 * C * 2, H // C, DH, PARTS, HALF), BF16, kind="Internal").ap()

        l_x = [sem(f"l_x{j}") for j in range(2)]
        l_w = {n: sem(f"l_{n}") for n in ("wk", "wq", "wv", "wo", "a", "b", "wr")}
        l_bkq = sem("l_bkq")
        l_bv = sem("l_bv")
        l_bo = sem("l_bo")
        l_br = sem("l_br")
        s_ident0 = sem("s_ident0")
        s_ident = sem("s_ident")
        s_const0 = sem("s_const0")
        s_causal = sem("s_causal")
        s_prio = sem("s_prio")
        s_wr0 = sem("s_wr0")
        s_vone = sem("s_vone")
        s_kone = sem("s_kone")
        s_veps = sem("s_veps")
        s_std = sem("s_std")
        s_nmr = sem("s_nmr")
        s_xn = sem("s_xn")
        s_bias = sem("s_bias")
        s_xb = sem("s_xb")
        filled = sem("filled")
        s_high = sem("s_high")
        read_act = sem("read_act")
        read_dve = sem("read_dve")
        freed = {"act": read_act, "dve": read_dve}
        s_part1 = sem("s_part1")
        s_parts = sem("s_parts")
        s_scr = [sem(f"s_scr{i}") for i in range(8)]
        s_stack = [sem(f"s_stack{i}") for i in range(8)]
        s_lm = sem("s_lm")
        s_ex = sem("s_ex")
        dve_chain = sem("dve_chain")
        mx_ready = sem("mx_ready")
        mx_taken = sem("mx_taken")
        m_split = sem("m_split")
        m_turned = sem("m_turned")
        m_row = sem("m_row")
        m_there = [sem(f"m_there{u}") for u in range(NU)]
        st_ready = sem("st_ready")
        exp_done = sem("exp_done")
        hidden = sem("hidden")
        pv_done = sem("pv_done")
        acc_taken = sem("acc_taken")
        acc_turned = sem("acc_turned")
        heads_there = sem("heads_there")
        hT_ready = sem("hT_ready")
        hT_taken = sem("hT_taken")
        o_ready = sem("o_ready")
        o_there = sem("o_there")
        s_out = sem("s_out")

        block = ctx.enter_context(nc.Block())

        xin = X.rearrange("b (t p) c -> p (b t) c", p=P)
        xout = out.rearrange("b (t p) c -> p (b t) c", p=P)

        @block.sync
        def _(sp):
            sp.dma_start(x_sb[:, 0:HB, :], xin[:, 0:HB, :]).then_inc(l_x[0], 16)
            for n, w in (("wk", Wk), ("wq", Wq)):
                sp.dma_start(w_raw[n], w.rearrange("(a p) c -> p a c", p=P)).then_inc(l_w[n], 16)
            for dst, b in ((bias_k, bk), (bias_q, bq)):
                sp.dma_start(dst[:], b.rearrange("(a p) -> p a", p=P), allow_slow_non_contiguous=True)\
                  .then_inc(l_bkq, 16)
            sp.dma_start(x_sb[:, HB:T, :], xin[:, HB:T, :]).then_inc(l_x[1], 16)
            sp.dma_start(wr_raw, Wr).then_inc(l_w["wr"], 16)
            sp.dma_start(br_all[:], br.partition_broadcast(P)).then_inc(l_br, 16)
            sp.dma_start(w_raw["wv"], Wv.rearrange("(a p) c -> p a c", p=P)).then_inc(l_w["wv"], 16)
            sp.dma_start(a_raw, A.rearrange("e r c -> (e r) c").rearrange("(a p) c -> p a c", p=P))\
              .then_inc(l_w["a"], 16)
            sp.dma_start(bv_all, bv.partition_broadcast(P)).then_inc(l_bv, 16)
            sp.dma_start(bo_all, bo.partition_broadcast(P)).then_inc(l_bo, 16)
            for a in range(C):
                sp.dma_start(b_raw[:, a], B[:, a * P:(a + 1) * P, :].rearrange("e p r -> p e r"))\
                  .then_inc(l_w["b"], 16)
            sp.dma_start(w_raw["wo"], Wo.rearrange("(a p) c -> p a c", p=P)).then_inc(l_w["wo"], 16)
            def to_scratch(i):
                w = kq_items[i][0]
                sp.wait_ge(s_parts, i + 1)
                to = scratch[i].rearrange("h d s n -> (h d) s n")
                src = parts[:, i % NPT]
                if w == "q":
                    for s0, n in ((0, 3), (3, 2), (5, 1)):
                        sp.dma_start(to[:, s0:s0 + n, :], src[:, 0:n, :]).then_inc(s_scr[i], 16)
                else:
                    for s0, p0, n in ((0, 0, 3), (3, 1, 2), (5, 2, 1)):
                        sp.dma_start(to[:, s0:s0 + n, :], src[:, p0:p0 + 1, :].broadcast_to([P, n, HALF]))\
                          .then_inc(s_scr[i], 16)

            def to_stack(i):
                w, c, j = kq_items[i]
                sp.wait_ge(s_scr[i], 48)
                sp.dma_start(stack[w][0:KR, c * 8:c * 8 + 8, j * HALF:(j + 1) * HALF],
                             scratch[i].rearrange("h d s n -> (d s) h n")).then_inc(s_stack[i], 16)

            def maximum_rows(u):
                g, j = units[u]
                sp.wait_ge(m_row, u + 1)
                for k in range(2):
                    sp.dma_start(stack["q"][KR + k:KR + k + 1, g * G:g * G + G, j * HALF:(j + 1) * HALF],
                                 mrow[k * G:(k + 1) * G, u % 2, :]).then_inc(m_there[u], 16)

            for what, i in dma_jobs:
                {"put": to_scratch, "get": to_stack, "m": maximum_rows}[what](i)
            for k in range(2 * NQ):
                q, j, c, t = share_of(k)
                if any(quarters[n][1] == j for n in range(q + 1, NQ)):
                    continue
                sp.wait_ge(o_there, k + 1)
                for b in (t, t + 1):
                    sp.wait_ge(read_dve, read_by(at_fill[("y", b)])[1])
                sp.dma_start(xout[:, t:t + 2, :], x_sb[:, t:t + 2, :]).then_inc(s_out, 16)
            sp.wait_ge(s_out, 16 * T // 2)

        @block.gpsimd
        def _(pool):
            nc.gpsimd.memset(ident[:], 0.0).then_inc(s_ident0, 1)
            pool.wait_ge(s_ident0, 1)
            nc.gpsimd.affine_select(out=ident[:], in_=ident[:], compare_op=ALU.not_equal, fill=1.0, base=0,
                                    pattern=[[-1, P]], channel_multiplier=1).then_inc(s_ident, 1)
            nc.gpsimd.memset(causal[:], 0.0).then_inc(s_const0, 1)
            pool.wait_ge(s_ident, 1)
            nc.gpsimd.tensor_copy(ident_bf[:], ident[:]).then_inc(s_ident, 1)
            pool.wait_ge(s_const0, 1)
            nc.gpsimd.affine_select(out=causal[:], in_=causal[:], compare_op=ALU.is_ge, fill=LOW,
                                    base=HALF - P, pattern=[[-1, HALF]], channel_multiplier=1)\
              .then_inc(s_causal, 1)
            nc.gpsimd.memset(wr_T[:], 0.0).then_inc(s_wr0, 1)
            for e in range(E):
                last = nc.gpsimd.memset(prio[:, e:e + 1], float(E - e))
            last.then_inc(s_prio, 1)
            pool.wait_ge(s_prio, 1)
            nc.gpsimd.memset(stack["k"][KR:MR, :, :], 1.0).then_inc(s_kone, 1)
            pool.wait_ge(s_kone, 1)
            nc.gpsimd.memset(v_aug[:, :, :, DH:VW], 0.0).then_inc(s_vone, 1)
            pool.wait_ge(s_vone, 1)
            nc.gpsimd.memset(v_aug[:, :, :, DH:DH + 1], 1.0).then_inc(s_vone, 1)
            pool.wait_ge(l_bo, 16)
            pool.wait_ge(s_xn, T)
            for t in range(T):
                last = nc.gpsimd.tensor_tensor(x_sb[:, t, :], x_sb[:, t, :], bo_all, ALU.add)
                last.then_inc(s_xb, 1)
            for s, (u, kb) in enumerate(steps):
                if diagonal[s]:
                    pool.wait_ge(exp_done, 2 * s + 2)
                    seen = prob[:, s % NP, :, 0:P]
                    nc.gpsimd.affine_select(out=seen, in_=seen, compare_op=ALU.is_ge, fill=0.0, base=0,
                                            pattern=[[0, G], [1, P]], channel_multiplier=-1)\
                      .then_inc(hidden, 1)

        @block.scalar
        def _(act):
            def take(f):
                act.wait_ge(filled, at_fill[f] + 1)
                return bank_of(at_fill[f])

            def copy_fill(f, dst):
                nc.scalar.copy(dst, take(f)[:, 0:dst.free_size()]).then_inc(read_act, 1)

            def std_of(j):
                act.wait_ge(s_veps, j + 1)
                nc.scalar.activation(std[:, j * HB:(j + 1) * HB], veps[:, j * HB:(j + 1) * HB], ACT.Sqrt)\
                  .then_inc(s_std, 1)

            def keys_queries(i):
                w, c, j = kq_items[i]
                src = take(("kq", i))
                if i == 0:
                    act.wait_ge(s_bias, 1)
                if i >= 2:
                    act.wait_ge(s_parts, i - 1)
                if i >= NPT:
                    act.wait_ge(s_scr[i - NPT], 48)
                nc.scalar.activation(full[:, i % 2, :], src, ACT.Identity, bias=half_bias[w][:, c:c + 1],
                                     scale=SCALE)
                nc.scalar.activation(parts[:, i % NPT, 0, :], src, ACT.Identity,
                                     bias=half_bias[w][:, c:c + 1], scale=SCALE).then_inc(read_act, 1)

            def maximum_rows(u):
                act.wait_ge(m_turned, u + 1)
                if u >= 2:
                    act.wait_ge(m_there[u - 2], 32)
                nc.scalar.copy(mrow[:, u % 2, :], misc[0:2 * G, 0:HALF // 2].bitcast(BF16)).then_inc(m_row, 1)

            def take_fill(f):
                what, i = f
                if what == "wo":
                    copy_fill(f, wo_T[:].rearrange("p c n -> p (c n)"))
                elif what == "kq":
                    keys_queries(i)
                elif what == "wr":
                    act.wait_ge(s_wr0, 1)
                    nc.scalar.copy(wr_T[:, :, 0:E], take(f)[:, 0:C * E].rearrange("p (c n) -> p c n", c=C))\
                      .then_inc(read_act, 1)
                elif what == "lt":
                    copy_fill(f, lgT)
                elif what == "bt":
                    copy_fill(f, b_T[:, 2 * i:2 * i + 2, :].rearrange("p c n -> p (c n)"))
                elif what == "ht":
                    if i >= 2:
                        act.wait_ge(filled, at_fill[("y", i - 2)] + 1)
                    copy_fill(f, hmT[:, i % 2].rearrange("p c n -> p (c n)"))

            def high_half(f):
                nc.scalar.copy(halves(f)[0], take(f)).then_inc(s_high, 1)

            def router_exp(_):
                act.wait_ge(s_lm, 1)
                nc.scalar.activation(ex[:], lg[:], ACT.Exp).then_inc(s_ex, 1)

            def accumulators(u):
                act.wait_ge(pv_done, last_step[u] + 1)
                if u == 0:
                    act.wait_ge(s_xb, T)
                    act.wait_ge(read_dve, read_by(at_fill[("v", 3)])[1])
                if u >= 2:
                    act.wait_ge(acc_turned, u - 1)
                nc.scalar.copy(acc_sb[:, u % 2, :], acc_bank[:]).then_inc(acc_taken, 1)

            def heads_turned(n):
                act.wait_ge(hT_ready, n + 1)
                if n >= 2:
                    act.wait_ge(o_ready, 2 * (n - 1))
                nc.scalar.copy(headsT[:, n % 2, :], misc[:]).then_inc(hT_taken, 1)

            def exponentials(k):
                s, hp = k
                u, kb = steps[s]
                w = HALF - P * max(0, kb - HB * units[u][1])
                act.wait_ge(st_ready, 2 * s + hp + 1)
                if s >= NP:
                    act.wait_ge(pv_done, s - NP + 1)
                nc.scalar.activation(prob[:, s % NP, 2 * hp:2 * hp + 2, 0:w], st[hp][:, :, 0:w], ACT.Exp)\
                  .then_inc(exp_done, 1)

            for what, k in act_jobs:
                {"std": std_of, "high": high_half, "fill": take_fill, "exp_router": router_exp, "m": maximum_rows,
                 "acc": accumulators, "hT": heads_turned, "exp": exponentials}[what](k)

        @block.vector
        def _(dve):
            chain = [0]

            def link(ins):
                chain[0] += 1
                ins.then_inc(dve_chain, 1)
                dve.wait_ge(dve_chain, chain[0])

            def take(f):
                dve.wait_ge(filled, at_fill[f] + 1)
                return bank_of(at_fill[f])

            def statistics(j):
                dve.wait_ge(l_x[j], 16)
                ts = range(j * HB, (j + 1) * HB)
                for t in ts:
                    last = nc.vector.bn_stats(stats[:, t, :], x_sb[:, t, :])
                link(last)
                for t in ts:
                    last = nc.vector.bn_aggr(mv[:, t, :], stats[:, t, :])
                link(last)
                r = slice(j * HB, (j + 1) * HB)
                nc.vector.tensor_scalar_add(veps[:, r], mv[:, r, 1], EPS).then_inc(s_veps, 1)
                if j == 0:
                    dve.wait_ge(l_bkq, 32)
                    nc.vector.tensor_scalar_mul(half_bias["k"][:], bias_k[:], SCALE)
                    nc.vector.tensor_scalar_mul(half_bias["q"][:], bias_q[:], SCALE).then_inc(s_bias, 1)

            def normalise_x(j):
                r = slice(j * HB, (j + 1) * HB)
                dve.wait_ge(s_std, j + 1)
                link(nc.vector.reciprocal(rstd[:, r], std[:, r]))
                link(nc.vector.scalar_tensor_tensor(nmr[:, r], mv[:, r, 0], -1.0, rstd[:, r], ALU.mult, ALU.mult))
                for t in range(j * HB, (j + 1) * HB):
                    nc.vector.tensor_scalar(xn_sb[:, t, :], x_sb[:, t, :], rstd[:, t:t + 1], nmr[:, t:t + 1],
                                            ALU.mult, ALU.add).then_inc(s_xn, 1)

            def low_half(f):
                high, low = halves(f)
                dve.wait_ge(s_high, split_fills.index(f) + 1)
                nc.vector.tensor_tensor(low, take(f), high.bitcast(F32), ALU.subtract).then_inc(read_dve, 1)

            def cut(i):
                slot = parts[:, i % NPT]
                dve.wait_ge(read_act, read_by(at_fill[("kq", i)])[1])
                link(nc.vector.tensor_tensor(rest[:, i % 2, :], full[:, i % 2, :], slot[:, 0, :], ALU.subtract))
                link(nc.vector.tensor_copy(slot[:, 1, :], rest[:, i % 2, :]))
                nc.vector.tensor_tensor(slot[:, 2, :], rest[:, i % 2, :], slot[:, 1, :], ALU.subtract)\
                  .then_inc(s_parts, 1)

            def router_logits():
                src = take(("lg", 0))[:, 0:2 * P].rearrange("p (b q e) -> p q b e", b=2, q=4)[:, :, :, 0:E]
                dve.wait_ge(l_br, 16)
                nc.vector.tensor_tensor(lg[:].rearrange("p (q b) e -> p q b e", b=2), src,
                                        br_all[:].unsqueeze(1).unsqueeze(1).broadcast_to([P, 4, 2, E]), ALU.add)\
                  .then_inc(read_dve, 1)
                dve.wait_ge(read_dve, read_by(at_fill[("lg", 0)])[1])
                link(nc.vector.reduce_max(r1[:], lg[:], AX.X))
                nc.vector.tensor_tensor(lg[:], lg[:], r1[:].unsqueeze(2).broadcast_to([P, T, E]), ALU.subtract)\
                  .then_inc(s_lm, 1)

            def router_choice():
                dve.wait_ge(s_ex, 1)
                dve.wait_ge(s_prio, 1)

                def each(r):
                    return r[:].unsqueeze(2).broadcast_to([P, T, E])
                link(nc.vector.reduce_sum(r1[:], ex[:], AX.X))
                link(nc.vector.reciprocal(r2[:], r1[:]))
                link(nc.vector.tensor_tensor(ex[:], ex[:], each(r2), ALU.mult))
                link(nc.vector.reduce_max(r3[:], ex[:], AX.X))
                nc.vector.tensor_scalar_mul(wgt[:], r3[:], 1.0 / R)
                link(nc.vector.tensor_tensor(cand[:], ex[:], each(r3), ALU.is_equal))
                link(nc.vector.tensor_tensor(cand[:], cand[:], prio[:].unsqueeze(1).broadcast_to([P, T, E]),
                                             ALU.mult))
                link(nc.vector.reduce_max(r1[:], cand[:], AX.X))
                link(nc.vector.tensor_tensor(onehot[:], cand[:], each(r1), ALU.is_equal))

            def values(i):
                src = take(("v", i)).rearrange("p (t h d) -> p t h d", t=2, d=DH)
                if i == 0:
                    dve.wait_ge(l_bv, 16)
                nc.vector.tensor_tensor(
                    v_aug[:, 2 * i:2 * i + 2, :, 0:DH], src,
                    bv_all.rearrange("p (h d) -> p h d", d=DH).unsqueeze(1).broadcast_to([P, 2, H, DH]),
                    ALU.add).then_inc(read_dve, 1)

            def chosen_rows(t):
                src = take(("h", t)).rearrange("p (e r) -> p e r", e=E)
                if t >= 2:
                    dve.wait_ge(filled, at_fill[("ht", t - 2)] + 1)
                nc.vector.tensor_tensor(hm[:, t % 2, :].rearrange("p (e r) -> p e r", e=E), src,
                                        onehot[:, t, :].unsqueeze(2).broadcast_to([P, E, R]), ALU.mult)\
                  .then_inc(read_dve, 1)

            def expert_out(t):
                src = take(("y", t))[:, 0:D]
                dve.wait_ge(s_xb, t + 1)
                before = [jk[0] for what, jk in dve_jobs[:dve_jobs.index(("y", (t,)))] if what == "out"]
                if before:
                    dve.wait_ge(o_there, before[-1] + 1)
                nc.vector.scalar_tensor_tensor(x_sb[:, t, :], src, wgt[:, t:t + 1], x_sb[:, t, :], ALU.mult, ALU.add)\
                  .then_inc(read_dve, 1)

            def maximum(i):
                u, qb, h, k0, w = mx_tiles[i]
                j = units[u][1]
                dve.wait_ge(mx_ready, i + 1)
                src = mx_bank[i % 2]
                b = qb - HB * j
                if i == 0:
                    dve.wait_ge(s_causal, 1)
                if j and k0 == 0:
                    nc.vector.reduce_max(pm[:, u % 2, 0, h, b:b + 1], src[:, 0:w], AX.X).then_inc(mx_taken, 1)
                else:
                    nc.vector.tensor_tensor_reduce(
                        out=masked[:, i % 2, 0:w], in0=src[:, 0:w], in1=causal[:, HALF - w:HALF], scale=1.0, scalar=LOW,
                        op0=ALU.add, op1=ALU.max, accum_out=pm[:, u % 2, 1, h, b:b + 1]).then_inc(mx_taken, 1)
                if i + 1 == mx_end[u]:
                    dve.wait_ge(mx_taken, i + 1)
                    m = pm[:, u % 2, 1]
                    if j:
                        link(nc.vector.tensor_tensor(m, pm[:, u % 2, 0], m, ALU.max))
                    if u >= 2:
                        dve.wait_ge(m_turned, u - 1)
                    part = [mpart[:, u % 2, :, k, :].rearrange("p b h -> p h b") for k in range(2)]
                    link(nc.vector.tensor_scalar_mul(part[0], m, -1.0))
                    nc.vector.scalar_tensor_tensor(part[1], m, -1.0, part[0],
                                                   ALU.mult, ALU.subtract).then_inc(m_split, 1)

            def normalise(u):
                g, j = units[u]
                dve.wait_ge(acc_turned, u + 1)
                src = misc[:].rearrange("p (b h w) -> p b h w", b=HB, h=G)
                link(nc.vector.reciprocal(rsum[:], src[:, :, :, DH]))
                nc.vector.tensor_tensor(
                    heads[:, j * HB:(j + 1) * HB, g * G * DH:(g + 1) * G * DH].rearrange("p b (h d) -> p b h d", h=G),
                    src[:, :, :, 0:DH], rsum[:].unsqueeze(3).broadcast_to([P, HB, G, DH]), ALU.mult)\
                  .then_inc(heads_there, 1)

            def result(k):
                t = share_of(k)[3]
                dve.wait_ge(o_ready, k + 1)
                if k == 0:
                    dve.wait_ge(s_xb, T)
                if k > 0:
                    dve.wait_ge(o_there, k)
                before = [jk[0] for what, jk in dve_jobs[:dve_jobs.index(("out", (k,)))] if what == "y"]
                if before:
                    dve.wait_ge(read_dve, read_by(at_fill[("y", before[-1])])[1])
                rows = x_sb[:, t:t + 2, :]
                nc.vector.tensor_tensor(rows, out_bank(k)[:].rearrange("p (t c) -> p t c", t=2), rows, ALU.add)\
                  .then_inc(o_there, 1)

            for what, k in dve_jobs:
                {"stats": statistics, "norm_x": normalise_x, "low": low_half, "cut": cut, "lg": router_logits,
                 "choice": router_choice, "v": values, "h": chosen_rows,
                 "y": expert_out, "mx": maximum, "norm": normalise, "out": result}[what](*k)

        @block.tensor
        def _(pe):
            def fill(f):
                i = at_fill[f]
                if i >= N_PRE:
                    free_misc(misc_uses.index(("fill", f)))
                elif i >= NB:
                    who, n = read_by(i - NB)
                    pe.wait_ge(freed[who], n)
                return bank_of(i)

            def product(dst, stationary, moving, part=slice(None)):
                terms = [(k, a, b) for k in range(C) for a, b in ((0, 0), (0, 1), (1, 0))]
                for n, (k, a, b) in list(enumerate(terms))[part]:
                    last = nc.tensor.matmul(dst, stationary(a, k), moving(b, k), start=n == 0, stop=n == len(terms) - 1)
                return last

            def turn(f, pairs):
                dst = fill(f)
                for k, (src, n) in enumerate(pairs):
                    last = nc.tensor.transpose(dst[:, k * n:k * n + n], src, ident[0:n, 0:n])
                last.then_inc(filled, 1)

            def read(f):
                who, n = read_by(at_fill[f])
                pe.wait_ge(freed[who], n)

            def do_fill(f):
                what, i = f
                if what in ("wk", "wq", "wv", "wo"):
                    pe.wait_ge(l_w[what], 16)
                    if f == fills[0]:
                        pe.wait_ge(s_ident, 1)
                    turn(f, [(w_raw[what][:, a, c * P:(c + 1) * P], P) for c in range(C) for a in range(C)])
                elif what == "x":
                    c, j = i % 2, i // 2
                    pe.wait_ge(s_xn, (j + 1) * HB)
                    turn(f, [(xn_sb[:, t, c * P:(c + 1) * P], P) for t in range(j * HB, (j + 1) * HB)])
                elif what == "wr":
                    pe.wait_ge(l_w["wr"], 16)
                    turn(f, [(wr_raw[:, c * P:(c + 1) * P], E) for c in range(C)])
                elif what == "at":
                    pe.wait_ge(l_w["a"], 16)
                    turn(f, [(a_raw[:, a, i * P:(i + 1) * P], P) for a in range(ERC)])
                elif what == "bt":
                    pe.wait_ge(l_w["b"], 32)
                    turn(f, [(b_raw[:, a, 2 * q:2 * q + 2, :].rearrange("p e r -> p (e r)"), P)
                             for q in (2 * i, 2 * i + 1) for a in range(C)])
                elif what == "kq":
                    kq_part(f, PARTS_OF["kq"] - 1 if at_fill[f] >= N_PRE else None).then_inc(filled, 1)
                elif what == "lt":
                    dst = fill(f)
                    read(("wr", 0))
                    read(("x", 3))
                    for n in range(2 * C):
                        x = xnT[n % 2][:, n // 2, :].bitcast(F32)
                        for q in range(4):
                            last = nc.tensor.matmul(dst[q * VW:(q + 1) * VW, 0:S // 4], wr_T[:, n // 2, :],
                                                    x[:, q * S // 4:(q + 1) * S // 4],
                                                    start=n == 0, stop=n == 2 * C - 1)
                    last.then_inc(filled, 1)
                elif what == "lg":
                    read(("lt", 0))
                    turn(f, [(lgT[:, b * P:(b + 1) * P], P) for b in range(2)])
                elif what == "v":
                    dst = fill(f)
                    read(("wv", 0))
                    for t in range(2):
                        b0 = (2 * i + t) * P
                        last = product(dst[:, t * D:(t + 1) * D], lambda a, k: xnT[a][:, k, b0:b0 + P],
                                       lambda b, k: w_T["wv"][b][:, k, :])
                    last.then_inc(filled, 1)
                elif what == "h":
                    h_part(f, PARTS_OF["h"] - 1).then_inc(filled, 1)
                elif what == "ht":
                    read(("h", i))
                    turn(f, [(hm[:, i % 2, q * P:(q + 1) * P], P) for q in range(ERC)])
                elif what == "y":
                    y_part(f, PARTS_OF["y"] - 1).then_inc(filled, 1)

            def kq_part(f, n):
                w, c, j = kq_items[f[1]]
                per = 3 * C // PARTS_OF["kq"]
                if not n:
                    fill(f)
                    read(("w" + w, 0))
                    read(("x", 2 * j + 1))
                return product(bank_of(at_fill[f]), lambda a, k: w_T["w" + w][a][:, k, c * P:(c + 1) * P],
                               lambda b, k: xnT[b][:, k, j * HALF:(j + 1) * HALF],
                               slice(None) if n is None else slice(n * per, (n + 1) * per))

            def h_part(f, n):
                t = f[1]
                per = 3 * C // PARTS_OF["h"]
                if n == 0:
                    fill(f)
                    read(("at", C - 1))
                return product(bank_of(at_fill[f]), lambda a, k: xnT[a][:, k, t * P:(t + 1) * P],
                               lambda b, k: a_T[b][:, k, :], slice(n * per, (n + 1) * per))

            def y_part(f, n):
                t = f[1]
                if n == 0:
                    fill(f)
                    read(("ht", t))
                    read(("bt", 1))
                per = ERC // PARTS_OF["y"]
                for q in range(n * per, (n + 1) * per):
                    last = nc.tensor.matmul(bank_of(at_fill[f])[:, 0:D], hmT[:, t % 2, q, :], b_T[:, q, :],
                                            start=q == 0, stop=q == ERC - 1)
                return last

            def fill_part(f, n):
                {"kq": kq_part, "h": h_part, "y": y_part}[f[0]](f, n)

            def mx(i):
                u, qb, h, k0, w = mx_tiles[i]
                g, j = units[u]
                if i >= 2:
                    pe.wait_ge(mx_taken, i - 1)
                if i == 0 or mx_tiles[i - 1][0] != u:
                    for n in stacks_of(u):
                        pe.wait_ge(s_stack[n], 16)
                hh = g * G + h
                nc.tensor.matmul(mx_bank[i % 2][:, 0:w], stack["q"][0:KR, hh, qb * P:(qb + 1) * P],
                                 stack["k"][0:KR, hh, k0:k0 + w], start=True, stop=True).then_inc(mx_ready, 1)

            def free_misc(n):
                if n == 0:
                    return
                what, k = misc_uses[n - 1]
                if what == "m":
                    pe.wait_ge(m_row, k + 1)
                elif what == "turn":
                    pe.wait_ge(heads_there, k + 1)
                elif what == "hT":
                    pe.wait_ge(hT_taken, k + 1)
                elif what == "fill":
                    read(k)
                else:
                    pe.wait_ge(o_there, k + 1)

            def m_turn(u):
                free_misc(misc_uses.index(("m", u)))
                pe.wait_ge(m_split, u + 1)
                if u == 0:
                    pe.wait_ge(s_ident, 2)
                for b in range(HB):
                    last = nc.tensor.transpose(misc[0:2 * G, b * P // 2:(b + 1) * P // 2].bitcast(BF16),
                                               mpart[:, u % 2, b].rearrange("p k h -> p (k h)"), ident_bf[:])
                last.then_inc(m_turned, 1)

            def acc_turn(u):
                free_misc(misc_uses.index(("turn", u)))
                pe.wait_ge(acc_taken, u + 1)
                for b in range(HB):
                    last = nc.tensor.transpose(misc[:, b * P:(b + 1) * P], acc_sb[:, u % 2, b * P:(b + 1) * P],
                                               ident[:])
                last.then_inc(acc_turned, 1)

            def hT(n):
                free_misc(misc_uses.index(("hT", n)))
                u, j, c = quarters[n]
                pe.wait_ge(heads_there, u + 1)
                for b in range(HB):
                    last = nc.tensor.transpose(misc[:, b * P:(b + 1) * P], heads[:, j * HB + b, c * P:(c + 1) * P],
                                               ident[:])
                last.then_inc(hT_ready, 1)

            def project(k):
                if ("out", k) in misc_uses:
                    free_misc(misc_uses.index(("out", k)))
                else:
                    pe.wait_ge(mx_taken, len(mx_tiles))
                n, j, c, t = share_of(k)
                pe.wait_ge(hT_taken, n + 1)
                for b in range(2):
                    q = t - j * HB + b
                    last = nc.tensor.matmul(out_bank(k)[:, b * D:(b + 1) * D], headsT[:, n % 2, q * P:(q + 1) * P],
                                            wo_T[:, c, :], start=True, stop=True)
                last.then_inc(o_ready, 1)

            def scores(s, hp):
                u, kb = steps[s]
                g, j = units[u]
                q0 = max(HALF * j, kb * P)
                w = HALF * (j + 1) - q0
                if s == first_step[u] and hp == 0:
                    pe.wait_ge(m_there[u], 32)
                if s >= 1:
                    pe.wait_ge(exp_done, 2 * (s - 1) + hp + 1)
                for h in range(2):
                    hh = g * G + 2 * hp + h
                    last = nc.tensor.matmul(st[hp][:, h, 0:w], stack["k"][0:MR, hh, kb * P:(kb + 1) * P],
                                            stack["q"][0:MR, hh, q0:q0 + w], start=True, stop=True)
                last.then_inc(st_ready, 1)

            def weigh(s):
                u, kb = steps[s]
                g, j = units[u]
                q0 = max(0, kb * P - HALF * j)
                pe.wait_ge(exp_done, 2 * s + 2)
                if diagonal[s]:
                    pe.wait_ge(hidden, hidden_before[s] + 1)
                if kb == 0 and u >= 1:
                    pe.wait_ge(acc_taken, u)
                for h in range(G):
                    last = nc.tensor.matmul(acc_bank[h * VW:(h + 1) * VW, q0:HALF], v_aug[:, kb, g * G + h, :],
                                            prob[:, s % NP, h, 0:HALF - q0], start=kb == 0, stop=s == last_step[u])
                last.then_inc(pv_done, 1)

            for what, k in pe_jobs:
                if (what, k) == ("st", (0, 0)):
                    for i in range(N_PRE - NB, N_PRE):
                        who, n = read_by(i)
                        pe.wait_ge(freed[who], n)
                    pe.wait_ge(s_vone, 2)
                    pe.wait_ge(s_kone, 1)
                {"fill": do_fill, "part": fill_part, "mx": mx, "m": m_turn, "turn": acc_turn, "hT": hT, "out": project,
                 "st": scores, "pv": weigh}[what](*k)


INS = ["L0_attn_X", "L0_attn_Wq", "L0_attn_bq", "L0_attn_Wk", "L0_attn_bk", "L0_attn_Wv", "L0_attn_bv", "L0_attn_Wo",
       "L0_attn_bo", "L0_ffn_A", "L0_ffn_B", "L0_ffn_Wr", "L0_ffn_br"]


def kernel(**inputs):
    import numpy as np
    import concourse.bacc as bacc
    from concourse.bass_utils import run_bass_kernel_spmd

    nc = bacc.Bacc("TRN2", target_bir_lowering=False, num_devices=1)
    arrays, args = {}, []
    for name in INS:
        a = np.ascontiguousarray(inputs[name])
        arrays[f"in_{name}"] = a
        args.append(nc.dram_tensor(f"in_{name}", a.shape, mybir.dt.from_np(a.dtype), kind="ExternalInput").ap())
    args.append(nc.dram_tensor("out_dram", inputs["L0_attn_X"].shape, F32, kind="ExternalOutput").ap())
    layer_kernel(nc, *args)
    r = run_bass_kernel_spmd(nc, [arrays], core_ids=[0])
    return r.results[0]["out_dram"]
```
